# Optimizing a Trainium2 kernel written in Bass

```python
import numpy as np
import jax
import jax.numpy as jnp

def _softmax(x, axis=-1):
    return jax.nn.softmax(x, axis=axis)

def _gelu(x):
    return jax.nn.gelu(x, approximate=True)

def _silu(x):
    return jax.nn.silu(x)

def _sigmoid(x):
    return jax.nn.sigmoid(x)

def _layernorm(x, axis=-1, eps=1e-05):
    m = jnp.mean(x, axis=axis, keepdims=True)
    v = jnp.var(x, axis=axis, keepdims=True)
    return (x - m) / jnp.sqrt(v + eps)

def _scatter_add(tgt, idx, src, axis=0):
    return tgt.at[idx].add(src)

def _segment_sum(src, seg, n):
    return jax.ops.segment_sum(src, seg, n)
kernel_name = 'mk_dlrm_tower_d1_rec_r8_e760a1'

def setup_inputs(seed: int=0):
    np.random.seed(seed)
    _w = jnp.asarray

    def _rec_inputs():
        import jax
        import jax.numpy as jnp
        _tk = jax.random.key(seed)
        dense_ctx = jax.random.normal(jax.random.fold_in(_tk, 190), (1024, 16), jnp.float32)
        ids = jnp.stack([jax.random.randint(jax.random.fold_in(_tk, 200 + f), (1024,), 0, v, jnp.int32) for f, v in enumerate([1000, 1000, 1000, 12500, 125000, 1250, 1250, 1000, 1250, 1250, 1250, 12500, 1250, 125000, 12500, 12500, 12500, 1250, 1250, 1000, 1250, 12500, 1000, 1250, 1000, 1250, 12500, 125000, 1000, 1250, 1250, 1250])], axis=1)
        tbl_0 = 0.05 * jax.random.normal(jax.random.fold_in(_tk, 500 + 0), (1000, 64), jnp.float32)
        tbl_1 = 0.05 * jax.random.normal(jax.random.fold_in(_tk, 500 + 1), (1000, 64), jnp.float32)
        tbl_2 = 0.05 * jax.random.normal(jax.random.fold_in(_tk, 500 + 2), (1000, 64), jnp.float32)
        tbl_3 = 0.05 * jax.random.normal(jax.random.fold_in(_tk, 500 + 3), (12500, 64), jnp.float32)
        tbl_4 = 0.05 * jax.random.normal(jax.random.fold_in(_tk, 500 + 4), (125000, 64), jnp.float32)
        tbl_5 = 0.05 * jax.random.normal(jax.random.fold_in(_tk, 500 + 5), (1250, 64), jnp.float32)
        tbl_6 = 0.05 * jax.random.normal(jax.random.fold_in(_tk, 500 + 6), (1250, 64), jnp.float32)
        tbl_7 = 0.05 * jax.random.normal(jax.random.fold_in(_tk, 500 + 7), (1000, 64), jnp.float32)
        tbl_8 = 0.05 * jax.random.normal(jax.random.fold_in(_tk, 500 + 8), (1250, 64), jnp.float32)
        tbl_9 = 0.05 * jax.random.normal(jax.random.fold_in(_tk, 500 + 9), (1250, 64), jnp.float32)
        tbl_10 = 0.05 * jax.random.normal(jax.random.fold_in(_tk, 500 + 10), (1250, 64), jnp.float32)
        tbl_11 = 0.05 * jax.random.normal(jax.random.fold_in(_tk, 500 + 11), (12500, 64), jnp.float32)
        tbl_12 = 0.05 * jax.random.normal(jax.random.fold_in(_tk, 500 + 12), (1250, 64), jnp.float32)
        tbl_13 = 0.05 * jax.random.normal(jax.random.fold_in(_tk, 500 + 13), (125000, 64), jnp.float32)
        tbl_14 = 0.05 * jax.random.normal(jax.random.fold_in(_tk, 500 + 14), (12500, 64), jnp.float32)
        tbl_15 = 0.05 * jax.random.normal(jax.random.fold_in(_tk, 500 + 15), (12500, 64), jnp.float32)
        tbl_16 = 0.05 * jax.random.normal(jax.random.fold_in(_tk, 500 + 16), (12500, 64), jnp.float32)
        tbl_17 = 0.05 * jax.random.normal(jax.random.fold_in(_tk, 500 + 17), (1250, 64), jnp.float32)
        tbl_18 = 0.05 * jax.random.normal(jax.random.fold_in(_tk, 500 + 18), (1250, 64), jnp.float32)
        tbl_19 = 0.05 * jax.random.normal(jax.random.fold_in(_tk, 500 + 19), (1000, 64), jnp.float32)
        tbl_20 = 0.05 * jax.random.normal(jax.random.fold_in(_tk, 500 + 20), (1250, 64), jnp.float32)
        tbl_21 = 0.05 * jax.random.normal(jax.random.fold_in(_tk, 500 + 21), (12500, 64), jnp.float32)
        tbl_22 = 0.05 * jax.random.normal(jax.random.fold_in(_tk, 500 + 22), (1000, 64), jnp.float32)
        tbl_23 = 0.05 * jax.random.normal(jax.random.fold_in(_tk, 500 + 23), (1250, 64), jnp.float32)
        tbl_24 = 0.05 * jax.random.normal(jax.random.fold_in(_tk, 500 + 24), (1000, 64), jnp.float32)
        tbl_25 = 0.05 * jax.random.normal(jax.random.fold_in(_tk, 500 + 25), (1250, 64), jnp.float32)
        tbl_26 = 0.05 * jax.random.normal(jax.random.fold_in(_tk, 500 + 26), (12500, 64), jnp.float32)
        tbl_27 = 0.05 * jax.random.normal(jax.random.fold_in(_tk, 500 + 27), (125000, 64), jnp.float32)
        tbl_28 = 0.05 * jax.random.normal(jax.random.fold_in(_tk, 500 + 28), (1000, 64), jnp.float32)
        tbl_29 = 0.05 * jax.random.normal(jax.random.fold_in(_tk, 500 + 29), (1250, 64), jnp.float32)
        tbl_30 = 0.05 * jax.random.normal(jax.random.fold_in(_tk, 500 + 30), (1250, 64), jnp.float32)
        tbl_31 = 0.05 * jax.random.normal(jax.random.fold_in(_tk, 500 + 31), (1250, 64), jnp.float32)
        _rk = jax.random.fold_in(_tk, 7)
        W_top1 = 0.0441942 * jax.random.normal(jax.random.fold_in(_tk, 801), (512, 512), jnp.float32)
        W_top2 = 0.0441942 * jax.random.normal(jax.random.fold_in(_tk, 802), (512, 256), jnp.float32)
        W_top3 = 0.0625 * jax.random.normal(jax.random.fold_in(_tk, 803), (256, 1), jnp.float32)
        b_top1 = jnp.zeros((512,), jnp.float32)
        b_top2 = jnp.zeros((256,), jnp.float32)
        return (dense_ctx, ids, tbl_0, tbl_1, tbl_2, tbl_3, tbl_4, tbl_5, tbl_6, tbl_7, tbl_8, tbl_9, tbl_10, tbl_11, tbl_12, tbl_13, tbl_14, tbl_15, tbl_16, tbl_17, tbl_18, tbl_19, tbl_20, tbl_21, tbl_22, tbl_23, tbl_24, tbl_25, tbl_26, tbl_27, tbl_28, tbl_29, tbl_30, tbl_31, W_top1, b_top1, W_top2, b_top2, W_top3)
    dense_ctx, ids, tbl_0, tbl_1, tbl_2, tbl_3, tbl_4, tbl_5, tbl_6, tbl_7, tbl_8, tbl_9, tbl_10, tbl_11, tbl_12, tbl_13, tbl_14, tbl_15, tbl_16, tbl_17, tbl_18, tbl_19, tbl_20, tbl_21, tbl_22, tbl_23, tbl_24, tbl_25, tbl_26, tbl_27, tbl_28, tbl_29, tbl_30, tbl_31, W_top1, b_top1, W_top2, b_top2, W_top3 = _rec_inputs()

    def _L0_rec_setup():
        import jax, jax.numpy as jnp
        import numpy as np
        FIELDS = 32
        EMBED = 64
        BATCH = 1024
        PAIR = FIELDS * (FIELDS - 1) // 2

        def _pair_ids(fields):
            pairs = np.array([(i, j) for i in range(fields - 1) for j in range(i + 1, fields)], dtype=np.int32)
            return (jnp.asarray(pairs[:, 0]), jnp.asarray(pairs[:, 1]))
        key = jax.random.key(seed)
        k1, k2 = jax.random.split(key)
        inputs = jax.random.normal(k1, (BATCH, FIELDS, EMBED), dtype=jnp.float32)
        w = 0.05 * jax.random.normal(k2, (PAIR, EMBED, EMBED), dtype=jnp.float32)
        return {'inputs': inputs, 'w': w}
    _L0_rec_all = _L0_rec_setup()
    _L0_rec_in = {k: v for k, v in _L0_rec_all.items() if k in ('w',)}
    del _L0_rec_all
    return {'dense_ctx': dense_ctx, 'ids': ids, 'tbl_0': tbl_0, 'tbl_1': tbl_1, 'tbl_2': tbl_2, 'tbl_3': tbl_3, 'tbl_4': tbl_4, 'tbl_5': tbl_5, 'tbl_6': tbl_6, 'tbl_7': tbl_7, 'tbl_8': tbl_8, 'tbl_9': tbl_9, 'tbl_10': tbl_10, 'tbl_11': tbl_11, 'tbl_12': tbl_12, 'tbl_13': tbl_13, 'tbl_14': tbl_14, 'tbl_15': tbl_15, 'tbl_16': tbl_16, 'tbl_17': tbl_17, 'tbl_18': tbl_18, 'tbl_19': tbl_19, 'tbl_20': tbl_20, 'tbl_21': tbl_21, 'tbl_22': tbl_22, 'tbl_23': tbl_23, 'tbl_24': tbl_24, 'tbl_25': tbl_25, 'tbl_26': tbl_26, 'tbl_27': tbl_27, 'tbl_28': tbl_28, 'tbl_29': tbl_29, 'tbl_30': tbl_30, 'tbl_31': tbl_31, 'W_top1': W_top1, 'b_top1': b_top1, 'W_top2': W_top2, 'b_top2': b_top2, 'W_top3': W_top3, 'L0_rec_w': _L0_rec_in['w']}

def reference(dense_ctx, ids, tbl_0, tbl_1, tbl_2, tbl_3, tbl_4, tbl_5, tbl_6, tbl_7, tbl_8, tbl_9, tbl_10, tbl_11, tbl_12, tbl_13, tbl_14, tbl_15, tbl_16, tbl_17, tbl_18, tbl_19, tbl_20, tbl_21, tbl_22, tbl_23, tbl_24, tbl_25, tbl_26, tbl_27, tbl_28, tbl_29, tbl_30, tbl_31, W_top1, b_top1, W_top2, b_top2, W_top3, L0_rec_w):
    import jax
    import jax.numpy as jnp

    def _L0_rec_ref(inputs, w):
        import jax, jax.numpy as jnp
        import numpy as np
        FIELDS = 32
        EMBED = 64
        BATCH = 1024
        PAIR = FIELDS * (FIELDS - 1) // 2

        def _pair_ids(fields):
            pairs = np.array([(i, j) for i in range(fields - 1) for j in range(i + 1, fields)], dtype=np.int32)
            return (jnp.asarray(pairs[:, 0]), jnp.asarray(pairs[:, 1]))
        ids_x, ids_y = _pair_ids(FIELDS)
        p = inputs[:, ids_x, :]
        q = inputs[:, ids_y, :]
        pw = jnp.einsum('bpi,pij->bpj', p, w)
        out = jnp.einsum('bpj,bpj->bp', pw, q)
        return out
    e = jnp.stack([tbl_0[ids[:, 0]], tbl_1[ids[:, 1]], tbl_2[ids[:, 2]], tbl_3[ids[:, 3]], tbl_4[ids[:, 4]], tbl_5[ids[:, 5]], tbl_6[ids[:, 6]], tbl_7[ids[:, 7]], tbl_8[ids[:, 8]], tbl_9[ids[:, 9]], tbl_10[ids[:, 10]], tbl_11[ids[:, 11]], tbl_12[ids[:, 12]], tbl_13[ids[:, 13]], tbl_14[ids[:, 14]], tbl_15[ids[:, 15]], tbl_16[ids[:, 16]], tbl_17[ids[:, 17]], tbl_18[ids[:, 18]], tbl_19[ids[:, 19]], tbl_20[ids[:, 20]], tbl_21[ids[:, 21]], tbl_22[ids[:, 22]], tbl_23[ids[:, 23]], tbl_24[ids[:, 24]], tbl_25[ids[:, 25]], tbl_26[ids[:, 26]], tbl_27[ids[:, 27]], tbl_28[ids[:, 28]], tbl_29[ids[:, 29]], tbl_30[ids[:, 30]], tbl_31[ids[:, 31]]], axis=1)
    z = _L0_rec_ref(e, L0_rec_w)
    z = z.reshape(z.shape[0], -1)
    h = jnp.concatenate([z, dense_ctx], axis=1)
    h = jnp.maximum(h @ W_top1 + b_top1, 0.0)
    h = jnp.maximum(h @ W_top2 + b_top2, 0.0)
    y = h @ W_top3
    return y

_drawn_inputs = setup_inputs


def setup_inputs(seed=0):
    import zlib

    import numpy as np

    out = dict(_drawn_inputs(seed))
    spreads = {'b_top1': (0.0, 0.1), 'b_top2': (0.0, 0.1)}
    factors = {'tbl_0': 6.501,
     'tbl_1': 5.968,
     'tbl_2': 5.791,
     'tbl_3': 5.427,
     'tbl_4': 4.961,
     'tbl_5': 6.49,
     'tbl_6': 5.802,
     'tbl_7': 5.008,
     'tbl_8': 5.6,
     'tbl_9': 5.824,
     'tbl_10': 5.786,
     'tbl_11': 5.262,
     'tbl_12': 5.217,
     'tbl_13': 5.163,
     'tbl_14': 5.799,
     'tbl_15': 5.619,
     'tbl_16': 5.125,
     'tbl_17': 6.087,
     'tbl_18': 5.061,
     'tbl_19': 5.75,
     'tbl_20': 5.258,
     'tbl_21': 5.324,
     'tbl_22': 5.897,
     'tbl_23': 5.896,
     'tbl_24': 5.653,
     'tbl_25': 5.573,
     'tbl_26': 5.782,
     'tbl_27': 5.623,
     'tbl_28': 6.027,
     'tbl_29': 5.853,
     'tbl_30': 5.813,
     'tbl_31': 6.111}
    for name, (base, spread) in spreads.items():
        noise = np.random.default_rng([zlib.crc32(name.encode()), seed]).standard_normal(out[name].shape)
        drawn = base * np.exp(spread * noise) if base else spread * noise
        out[name] = jnp.asarray(drawn.astype(out[name].dtype))
    for name, factor in factors.items():
        out[name] = (out[name] * factor).astype(out[name].dtype)
    return out
```

```python
from contextlib import ExitStack

import concourse.bass as bass
from concourse import mybir

FIELDS, EMBED, BATCH, DENSE = 32, 64, 1024, 16
PAIRS = FIELDS * (FIELDS - 1) // 2
P = 128
COLS = 512
PASSES = BATCH // COLS
CHUNKS = COLS // P
COUPLES = FIELDS // 2
TILES = COUPLES * COUPLES
QUAD = 4
QUADS = TILES // QUAD
DUOS = TILES // 2
BLOCK = 16
BLOCKS = QUADS // BLOCK
H1, H2 = 512, 256
MLP_DUOS = 4
SLOTS = DUOS + MLP_DUOS
PS_BUFS = 3
W_RING = 4
S_RING = 4
Q_RING = 4
PROD_RING = 2
LOOKAHEAD = 2


def tile_of(t):
    j = int(t ** 0.5 + 1e-9)
    return t - j * j, j


def first_duo(j):
    return j * j // 2


def transpose_at(j):
    return max(0, first_duo(j) - LOOKAHEAD)


def nth(h, n, per_pass):
    return h * per_pass + (per_pass + n)


def build(nc, out, ids, tables, wtiles, wtop1, btop1, wtop2, btop2, wtop3, dense_rows, eye, ones):
    f32, f32r, i32 = mybir.dt.float32, mybir.dt.float32r, mybir.dt.int32
    u32 = mybir.dt.uint32
    ALU = mybir.AluOpType
    ACT = mybir.ActivationFunctionType
    ctx = ExitStack()
    with ctx:
        def sb(name, shape, dt=f32):
            return ctx.enter_context(nc.sbuf_tensor(name, shape, dt))

        def ps(name, shape):
            return ctx.enter_context(nc.psum_tensor(name, shape, f32))

        def sem(name):
            return ctx.enter_context(nc.semaphore(name))

        rows = sb("rows", [P, COUPLES, CHUNKS, 2 * EMBED])
        xs = sb("xs", [P, FIELDS, COLS], f32r)
        qs = sb("qs", [P, Q_RING, COLS])
        wraw = sb("wraw", [P, W_RING, QUAD * P])
        whigh = sb("whigh", [P, S_RING, QUAD * P], f32r)
        wlow = sb("wlow", [P, S_RING, QUAD * P], f32r)
        prod = sb("prod", [P, PROD_RING * QUAD, COLS])
        zs = sb("zs", [P, BLOCKS, COLS])
        h1s = sb("h1s", [P, H1 // P, COLS])
        h2s = sb("h2s", [P, H2 // P, COLS])
        ys = sb("ys", [1, BATCH])
        wt1 = sb("wt1", [P, BLOCKS, H1])
        wt2 = sb("wt2", [P, H1 // P, H2])
        wt3 = sb("wt3", [P, H2 // P])
        b1 = sb("b1", [P, H1 // P])
        b2 = sb("b2", [P, H2 // P])
        idx = sb("idx", [P, PASSES * COUPLES * CHUNKS * 2], i32)
        ident = sb("ident", [P, P])
        window = sb("window", [P, 62])

        pbuf = ps("pbuf", [P, 2 * PS_BUFS, COLS])
        zacc = ps("zacc", [P, COLS])
        tps = ps("tps", [P, COLS])

        ids_loaded = sem("ids_loaded")
        consts_loaded = sem("consts_loaded")
        mlp_loaded = sem("mlp_loaded")
        gathered = [sem(f"gathered{j}") for j in range(COUPLES)]
        raw_loaded = [sem(f"raw_loaded{s}") for s in range(W_RING)]
        transposed = sem("transposed")
        x_high = sem("x_high")
        x_ready = sem("x_ready")
        w_high = sem("w_high")
        w_ready = sem("w_ready")
        products = sem("products")
        drained = sem("drained")
        summed = sem("summed")
        z_ready = sem("z_ready")
        dense_loaded = sem("dense_loaded")
        y_stored = sem("y_stored")

        block = ctx.enter_context(nc.Block())

        @block.sync
        def _(sp):
            sp.dma_start(idx[:], ids).then_inc(ids_loaded, 16)
            sp.dma_start(ident[:], eye).then_inc(consts_loaded, 16)
            sp.dma_start(window[:], ones).then_inc(consts_loaded, 16)
            with sp.Fori(0, PASSES) as h:
                for q in range(QUADS):
                    slot = q % W_RING
                    sp.wait_ge(w_ready, nth(h, q - W_RING + 1, QUADS))
                    for half in range(2):
                        sp.dma_start(wraw[EMBED * half:EMBED * (half + 1), slot, :],
                                     wtiles[q]).then_inc(raw_loaded[slot], 16)
                    if q == 8:
                        sp.wait_ge(products, nth(h, DUOS + 2 - SLOTS, SLOTS))
                        sp.dma_start(zs[:], dense_rows[bass.ds(h, 1)].rearrange("o p b c -> (o p) b c")
                                     ).then_inc(dense_loaded, 16)
            sp.wait_ge(drained, SLOTS * (PASSES + 1))
            sp.dma_start(out, ys[:]).then_inc(y_stored, 16)
            sp.wait_ge(y_stored, 16)

        @block.gpsimd
        def _(pool):
            pool.wait_ge(ids_loaded, 16)
            for h in range(PASSES):
                for j in range(COUPLES):
                    pool.wait_ge(transposed, nth(h, j + 1 - COUPLES, COUPLES))
                    for c in range(CHUNKS):
                        for f in range(2):
                            n = ((h * COUPLES + j) * CHUNKS + c) * 2 + f
                            pool.indirect_dma_start(
                                rows[:, j, c, f * EMBED:(f + 1) * EMBED], None, tables[2 * j + f],
                                bass.IndirectOffsetOnAxis(ap=idx[:, n:n + 1].bitcast(u32), axis=0),
                            ).then_inc(gathered[j], 16)

        @block.scalar
        def _(act):
            act.dma_start(wt1[:], wtop1).then_inc(mlp_loaded, 16)
            act.dma_start(wt2[:], wtop2).then_inc(mlp_loaded, 16)
            act.dma_start(wt3[:], wtop3).then_inc(mlp_loaded, 16)
            act.dma_start(b1[:], btop1).then_inc(mlp_loaded, 16)
            act.dma_start(b2[:], btop2).then_inc(mlp_loaded, 16)
            act.sem_inc(w_high, QUADS)
            act.sem_inc(x_high, COUPLES)

            def high_halves_of_quad(h, q):
                slot = q % W_RING
                act.wait_ge(raw_loaded[slot], h * (32 * QUADS // W_RING) + 32 * (q // W_RING + 1))
                act.wait_ge(products, nth(h, before(2 * (q - S_RING) + 2), SLOTS))
                nc.scalar.activation(whigh[:, q % S_RING, :], wraw[:, slot, :], ACT.Copy).then_inc(w_high, 1)

            def before(n):
                return n if n > 0 else n - MLP_DUOS

            def high_halves_of_couple(h, j):
                act.wait_ge(transposed, nth(h, j + 1, COUPLES))
                if j >= Q_RING:
                    act.wait_ge(drained, nth(h, first_duo(j - Q_RING + 1) + 1, SLOTS))
                else:
                    act.wait_ge(drained, nth(h, 0, SLOTS))
                nc.scalar.activation(qs[:, j % Q_RING, :], tps[:], ACT.Copy)
                last = ((COUPLES - 1) ** 2 + min(2 * j + 1, 2 * COUPLES - 2)) // 2 + 1
                act.wait_ge(products, nth(h, last - SLOTS, SLOTS))
                for f in range(2):
                    a = EMBED * f
                    done = nc.scalar.activation(xs[a:a + EMBED, 2 * j + f, :], tps[a:a + EMBED, :], ACT.Copy)
                done.then_inc(x_high, 1)

            with act.Fori(0, PASSES) as h:
                for q in range(QUADS + S_RING):
                    for j in range(COUPLES):
                        if transpose_at(j) // 2 + S_RING == q:
                            high_halves_of_couple(h, j)
                    if q < QUADS:
                        high_halves_of_quad(h, q)

        @block.vector
        def _(dve):
            dve.sem_inc(x_ready, COUPLES)
            dve.sem_inc(w_ready, QUADS)
            dve.sem_inc(drained, SLOTS)
            dve.sem_inc(z_ready, BLOCKS)
            dve.wait_ge(mlp_loaded, 5 * 16)

            def low_halves_of_quad(h, q):
                dve.wait_ge(w_high, nth(h, q + 1, QUADS))
                nc.vector.tensor_tensor(wlow[:, q % S_RING, :], wraw[:, q % W_RING, :],
                                        whigh[:, q % S_RING, :].bitcast(f32), ALU.subtract).then_inc(w_ready, 1)

            def low_halves_of_couple(h, j):
                dve.wait_ge(x_high, nth(h, j + 1, COUPLES))
                for f in range(2):
                    a, b = EMBED * f, EMBED * (1 - f)
                    done = nc.vector.tensor_tensor(xs[b:b + EMBED, 2 * j + f, :], tps[a:a + EMBED, :],
                                                   xs[a:a + EMBED, 2 * j + f, :].bitcast(f32), ALU.subtract)
                done.then_inc(x_ready, 1)

            def multiply_duo(h, d):
                dve.wait_ge(products, nth(h, d + 1, SLOTS))
                dve.wait_ge(summed, nth(h, d // 2 + 1 - PROD_RING, QUADS))
                at, to = d % PS_BUFS * 2, d % (2 * PROD_RING) * 2
                ja, jb = tile_of(2 * d)[1] % Q_RING, tile_of(2 * d + 1)[1] % Q_RING
                if ja == jb:
                    q = qs[:, ja:ja + 1, :].to_broadcast([P, 2, COLS])
                    nc.vector.tensor_tensor(prod[:, to:to + 2, :], pbuf[:, at:at + 2, :], q,
                                            ALU.mult).then_inc(drained, 1)
                else:
                    nc.vector.tensor_tensor(prod[:, to, :], pbuf[:, at, :], qs[:, ja, :], ALU.mult)
                    nc.vector.tensor_tensor(prod[:, to + 1, :], pbuf[:, at + 1, :], qs[:, jb, :],
                                            ALU.mult).then_inc(drained, 1)

            def keep_block(h, b):
                dve.wait_ge(summed, nth(h, BLOCK * (b + 1), QUADS))
                if b == 0:
                    dve.wait_ge(dense_loaded, h * 16 + 16)
                nc.vector.tensor_tensor(zs[:, b, :], zacc[:], zs[:, b, :], ALU.add).then_inc(z_ready, 1)

            def relu_duo(h, n, to, bias):
                dve.wait_ge(products, nth(h, DUOS + n + 1, SLOTS))
                for m in range(2):
                    at = (DUOS + n) % PS_BUFS * 2 + m
                    done = nc.vector.tensor_scalar(to[:, m, :], pbuf[:, at, :], bias[:, m:m + 1], 0.0,
                                                   ALU.add, ALU.max)
                done.then_inc(drained, 1)

            with dve.Fori(0, PASSES) as h:
                for q in range(S_RING):
                    low_halves_of_quad(h, q)
                for d in range(DUOS):
                    for j in range(COUPLES):
                        if min(transpose_at(j) + 1, first_duo(j)) == d:
                            low_halves_of_couple(h, j)
                    multiply_duo(h, d)
                    q = d // 2
                    if d % 2 == 0 and q >= 1 and q + S_RING - 1 < QUADS:
                        low_halves_of_quad(h, q + S_RING - 1)
                    if d % 2 and q and q % BLOCK == 0:
                        keep_block(h, q // BLOCK - 1)
                keep_block(h, BLOCKS - 1)
                relu_duo(h, 0, h1s[:, 0:2, :], b1[:, 0:2])
                relu_duo(h, 1, h1s[:, 2:4, :], b1[:, 2:4])
                relu_duo(h, 2, h2s, b2)
                dve.wait_ge(products, nth(h, SLOTS, SLOTS))
                nc.vector.tensor_copy(ys[:, bass.ds(h * COLS, COLS)], pbuf[0:1, (SLOTS - 1) % PS_BUFS * 2, :]).then_inc(drained, 1)

        @block.tensor
        def _(pe):
            pe.sem_inc(transposed, COUPLES)
            pe.sem_inc(products, SLOTS)
            pe.sem_inc(summed, QUADS)
            pe.wait_ge(consts_loaded, 2 * 16)
            pe.wait_ge(mlp_loaded, 5 * 16)

            def transpose_couple(h, j):
                pe.wait_ge(gathered[j], (h + 1) * (16 * 2 * CHUNKS))
                pe.wait_ge(x_ready, nth(h, j, COUPLES))
                for c in range(CHUNKS):
                    done = nc.tensor.transpose(tps[:, c * P:(c + 1) * P], rows[:, j, c, :], ident[:])
                done.then_inc(transposed, 1)

            def products_of_duo(h, d):
                if d % 2 == 0:
                    pe.wait_ge(w_ready, nth(h, d // 2 + 1, QUADS))
                pe.wait_ge(drained, nth(h, d + 1 - PS_BUFS, SLOTS))
                for t in range(2 * d, 2 * d + 2):
                    i, j = tile_of(t)
                    if i == 2 * j:
                        pe.wait_ge(x_ready, nth(h, j + 1, COUPLES))
                    at = slice(t % QUAD * P, (t % QUAD + 1) * P)
                    to = pbuf[:, d % PS_BUFS * 2 + t % 2, :]
                    nc.tensor.matmul(to, whigh[:, t // QUAD % S_RING, at], xs[:, i, :], start=True, stop=False)
                    done = nc.tensor.matmul(to, wlow[:, t // QUAD % S_RING, at], xs[:, i, :],
                                            start=False, stop=True)
                done.then_inc(products, 1)

            def sum_quad(h, q):
                pe.wait_ge(drained, nth(h, 2 * q + 2, SLOTS))
                k = q % BLOCK
                if k == 0:
                    pe.wait_ge(z_ready, nth(h, q // BLOCK, BLOCKS))
                for g in range(QUAD):
                    done = nc.tensor.matmul(zacc[32 * g:32 * (g + 1), :], window[:, 30 - 2 * k:62 - 2 * k],
                                            prod[:, q % PROD_RING * QUAD + g, :],
                                            start=(k == 0), stop=(k == BLOCK - 1))
                done.then_inc(summed, 1)

            def layer(n, m, weights, inputs, kbs, first, last):
                for kb in kbs:
                    done = nc.tensor.matmul(pbuf[:, (DUOS + n) % PS_BUFS * 2 + m % 2, :],
                                            weights[:, kb, m * P:(m + 1) * P], inputs[:, kb, :],
                                            start=(kb == first), stop=(kb == last))
                return done

            with pe.Fori(0, PASSES) as h:
                for d in range(DUOS):
                    for j in range(COUPLES):
                        if transpose_at(j) == d:
                            transpose_couple(h, j)
                    products_of_duo(h, d)
                    if d % 2 and d > 1:
                        sum_quad(h, d // 2 - 1)
                last = BLOCKS - 1
                pe.wait_ge(drained, nth(h, DUOS + 1 - PS_BUFS, SLOTS))
                pe.wait_ge(z_ready, nth(h, last, BLOCKS))
                for m in range(2):
                    layer(0, m, wt1, zs, range(last), 0, last)
                sum_quad(h, QUADS - 1)
                pe.wait_ge(drained, nth(h, DUOS + 2 - PS_BUFS, SLOTS))
                for m in range(2, 4):
                    layer(1, m, wt1, zs, range(last), 0, last)
                pe.wait_ge(z_ready, nth(h, BLOCKS, BLOCKS))
                for n in range(2):
                    for m in range(2 * n, 2 * n + 2):
                        done = layer(n, m, wt1, zs, [last], 0, last)
                    done.then_inc(products, 1)
                pe.wait_ge(drained, nth(h, DUOS + 1, SLOTS))
                for m in range(2):
                    layer(2, m, wt2, h1s, [0, 1], 0, 3)
                pe.wait_ge(drained, nth(h, DUOS + 2, SLOTS))
                for m in range(2):
                    done = layer(2, m, wt2, h1s, [2, 3], 0, 3)
                done.then_inc(products, 1)
                pe.wait_ge(drained, nth(h, DUOS + 3, SLOTS))
                for kb in range(2):
                    done = nc.tensor.matmul(pbuf[0:1, (SLOTS - 1) % PS_BUFS * 2, :], wt3[:, kb:kb + 1],
                                            h2s[:, kb, :], start=(kb == 0), stop=(kb == 1))
                done.then_inc(products, 1)


def kernel(**inputs):
    import numpy as np
    import concourse.bacc as bacc
    from concourse import mybir as mb
    from concourse.bass_utils import run_bass_kernel_spmd

    w = np.asarray(inputs["L0_rec_w"])
    ids = np.asarray(inputs["ids"])
    dense = np.asarray(inputs["dense_ctx"])
    wtop1 = np.asarray(inputs["W_top1"])
    pair, n = {}, 0
    for i in range(FIELDS - 1):
        for j in range(i + 1, FIELDS):
            pair[i, j] = n
            n += 1
    wtiles = np.zeros((QUADS, EMBED, QUAD, 2, EMBED), np.float32)
    wt1 = np.zeros((P, BLOCKS, H1), np.float32)
    dense_rows = np.zeros((PASSES, P, BLOCKS, COLS), np.float32)
    for t in range(TILES):
        i, j = tile_of(t)
        q, g = t // QUAD, t % QUAD
        for s in range(2):
            row, b = 32 * g + 2 * (q % BLOCK) + s, q // BLOCK
            if 2 * j + s > i:
                wtiles[q, :, g, s] = w[pair[i, 2 * j + s]]
                wt1[row, b] = wtop1[pair[i, 2 * j + s]]
            else:
                wt1[row, b] = wtop1[PAIRS + j]
                for h in range(PASSES):
                    dense_rows[h, row, b] = dense[h * COLS:(h + 1) * COLS, j]
    window = np.zeros((P, 62), np.float32)
    window[:EMBED, 30] = 1
    window[EMBED:, 31] = 1
    arrays = {
        "ids_d": ids.reshape(PASSES, CHUNKS, P, COUPLES, 2).transpose(2, 0, 3, 1, 4).reshape(P, -1),
        "wtiles_d": wtiles.reshape(QUADS, EMBED, QUAD * P),
        "wtop1_d": wt1,
        "btop1_d": np.asarray(inputs["b_top1"]).reshape(H1 // P, P).T,
        "wtop2_d": np.asarray(inputs["W_top2"]).reshape(H1 // P, P, H2).transpose(1, 0, 2),
        "btop2_d": np.asarray(inputs["b_top2"]).reshape(H2 // P, P).T,
        "wtop3_d": np.asarray(inputs["W_top3"]).reshape(H2 // P, P).T,
        "dense_d": dense_rows,
        "eye_d": np.eye(P, dtype=np.float32),
        "window_d": window,
    }
    for f in range(FIELDS):
        arrays[f"tbl_{f}_d"] = np.asarray(inputs[f"tbl_{f}"])
    arrays = {k: np.ascontiguousarray(v) for k, v in arrays.items()}

    nc = bacc.Bacc("TRN2", target_bir_lowering=False, num_devices=1)
    ap = {k: nc.dram_tensor(k, v.shape, mb.dt.from_np(v.dtype), kind="ExternalInput").ap()
          for k, v in arrays.items()}
    out = nc.dram_tensor("y_d", (1, BATCH), mb.dt.float32, kind="ExternalOutput").ap()
    build(nc, out, ap["ids_d"], [ap[f"tbl_{f}_d"] for f in range(FIELDS)], ap["wtiles_d"], ap["wtop1_d"],
          ap["btop1_d"], ap["wtop2_d"], ap["btop2_d"], ap["wtop3_d"], ap["dense_d"], ap["eye_d"],
          ap["window_d"])
    r = run_bass_kernel_spmd(nc, [arrays], core_ids=[0])
    return r.results[0]["y_d"].reshape(BATCH, 1)
```

```python
from contextlib import ExitStack

import concourse.bass as bass
from concourse import mybir

FIELDS, EMBED, BATCH, DENSE = 32, 64, 1024, 16
PAIRS = FIELDS * (FIELDS - 1) // 2
P = 128
COLS = 512
PASSES = BATCH // COLS
CHUNKS = COLS // P
COUPLES = FIELDS // 2
TILES = COUPLES * COUPLES
QUAD = 4
QUADS = TILES // QUAD
DUOS = TILES // 2
BLOCK = 16
BLOCKS = QUADS // BLOCK
H1, H2 = 512, 256
MLP_DUOS = 4
SLOTS = DUOS + MLP_DUOS
PS_BUFS = 3
W_RING = 4
S_RING = 4
Q_RING = 4
POOL_SLACK = 2.0
APART = 5
SECOND_FIELD = 3
GATHER_SLACK = 4.0
PROD_RING = 4
SUM_QUADS = 2
ROWS_RING = 8
K_ROWS = 125
K_TILES = 8
LOOKAHEAD = 2
AHEAD = 2


SMALL = [0, 1, 2, 7]
ORDER = SMALL + [f for f in range(FIELDS) if f not in SMALL]


def tile_of(t):
    j = int(t ** 0.5 + 1e-9)
    return t - j * j, j


def first_duo(j):
    return j * j // 2


def couples_at(d):
    at = {j: max(0, first_duo(j) - LOOKAHEAD) for j in range(AHEAD, COUPLES)}
    for n in range(AHEAD):
        at[COUPLES + n] = DUOS - 4 * (AHEAD - n)
    return [j for j in at if at[j] == d]


def pool_order():
    GATHER, LOW, QUAD_US, MLP_US, START, SLACK = 1.04, 1.25, 2.9, 22.0, 22.0, POOL_SLACK

    def at(h, q):
        return START + QUAD_US * q + (QUADS * QUAD_US + MLP_US) * h

    gathers = [(h, j, c, f) for h in range(PASSES) for j in range(AHEAD * (h == 0), COUPLES)
               for c in range(CHUNKS) for f in range(2)]

    def spare(now):
        least, n = 1e9, 0
        for h, j, c, f in gathers:
            n += 1
            if c == CHUNKS - 1 and f:
                early = (first_duo(j) - LOOKAHEAD) / 2 if j >= AHEAD else -6
                least = min(least, at(h, early) - GATHER_SLACK - now - n * GATHER)
        return least

    order, now, next_quad = [], 0.0, (0, S_RING)
    while gathers or next_quad[0] < PASSES:
        h, q = next_quad
        if h < PASSES and now + LOW > at(h, q) - SLACK:
            next_quad = (h, q + 1) if q + 1 < QUADS else (h + 1, 0)
        elif h < PASSES and now >= at(h, q - S_RING) + 2 and spare(now) > LOW:
            order.append((h, q))
            now += LOW
            next_quad = (h, q + 1) if q + 1 < QUADS else (h + 1, 0)
        elif gathers:
            order.append(gathers.pop(0))
            now += GATHER
        else:
            now += 0.5
    return order


def nth(h, n, per_pass):
    return h * per_pass + (per_pass + n)


def build(nc, out, ids, tables, wtiles, wtop1, btop1, wtop2, btop2, wtop3, dense_rows, eye, ones,
          small_ids, row_numbers):
    f32, f32r, i32 = mybir.dt.float32, mybir.dt.float32r, mybir.dt.int32
    u32 = mybir.dt.uint32
    ALU = mybir.AluOpType
    ACT = mybir.ActivationFunctionType
    ctx = ExitStack()
    with ctx:
        def sb(name, shape, dt=f32):
            return ctx.enter_context(nc.sbuf_tensor(name, shape, dt))

        def ps(name, shape):
            return ctx.enter_context(nc.psum_tensor(name, shape, f32))

        def sem(name):
            return ctx.enter_context(nc.semaphore(name))

        rows = sb("rows", [P, ROWS_RING, CHUNKS, 2 * EMBED])
        xs = sb("xs", [P, FIELDS, COLS], f32r)
        qs = sb("qs", [P, Q_RING, COLS])
        wraw = sb("wraw", [P, W_RING, QUAD * P])
        whigh = sb("whigh", [P, S_RING, QUAD * P], f32r)
        wlow = sb("wlow", [P, S_RING, QUAD * P], f32r)
        prod = sb("prod", [P, PROD_RING * QUAD, COLS])
        zs = sb("zs", [P, BLOCKS, COLS])
        h1s = sb("h1s", [P, H1 // P, COLS])
        h2s = sb("h2s", [P, H2 // P, COLS])
        ys = sb("ys", [1, BATCH])
        wt1 = sb("wt1", [P, BLOCKS, H1])
        wt2 = sb("wt2", [P, H1 // P, H2])
        wt3 = sb("wt3", [P, H2 // P])
        b1 = sb("b1", [P, H1 // P])
        b2 = sb("b2", [P, H2 // P])
        idx = sb("idx", [P, PASSES * COUPLES * CHUNKS * 2], i32)
        ident = sb("ident", [P, P])
        first_ids = h1s[:, :, :].bitcast(i32)
        numbers = sb("numbers", [P, K_TILES])
        table_slot = ROWS_RING - 2 * AHEAD
        window = sb("window", [P, 62])

        pbuf = ps("pbuf", [P, 2 * PS_BUFS, COLS])
        zacc = ps("zacc", [P, COLS])
        tps = ps("tps", [P, COLS])

        ids_loaded = sem("ids_loaded")
        consts_loaded = sem("consts_loaded")
        mlp_loaded = sem("mlp_loaded")
        numbers_loaded = sem("numbers_loaded")
        small_loaded = [sem(f"small_loaded{n}") for n in range(2 * AHEAD)]
        one_hot = sem("one_hot")
        looked_up = sem("looked_up")
        gathered = [sem(f"gathered{j}") for j in range(COUPLES)]
        raw_loaded = [sem(f"raw_loaded{s}") for s in range(W_RING)]
        transposed = sem("transposed")
        x_high = sem("x_high")
        x_ready = sem("x_ready")
        w_high = sem("w_high")
        w_ready = [sem(f"w_ready{s}") for s in range(S_RING)]
        products = sem("products")
        drained = sem("drained")
        mlp_drained = sem("mlp_drained")
        summed = sem("summed")
        z_ready = sem("z_ready")
        dense_loaded = sem("dense_loaded")
        y_stored = sem("y_stored")

        def wait_low(eng, h, q):
            eng.wait_ge(w_ready[q % S_RING], nth(h, q // S_RING + 1, QUADS // S_RING))

        block = ctx.enter_context(nc.Block())

        @block.sync
        def _(sp):
            sp.dma_start(idx[:], ids).then_inc(ids_loaded, 16)
            sp.dma_start(numbers[:], row_numbers).then_inc(numbers_loaded, 16)

            def load_quad(q):
                for half in range(2):
                    sp.dma_start(wraw[EMBED * half:EMBED * (half + 1), q % W_RING, :],
                                 wtiles[q % QUADS]).then_inc(raw_loaded[q % W_RING], 16)

            for n in range(2 * AHEAD):
                sp.dma_start(first_ids[:, n, :], small_ids[n:n + 1].to_broadcast([P, COLS])
                             ).then_inc(small_loaded[n], 16)
                sp.dma_start(rows[0:K_ROWS, table_slot + n, :, :].rearrange("p a b -> p (a b)"),
                             tables[n].rearrange("(p t) e -> p (t e)", t=K_TILES)
                             ).then_inc(small_loaded[n], 16)
            for q in range(W_RING):
                load_quad(q)
            sp.dma_start(ident[:], eye).then_inc(consts_loaded, 16)
            sp.dma_start(window[:], ones).then_inc(consts_loaded, 16)
            for to, of in ((wt1, wtop1), (wt2, wtop2), (wt3, wtop3), (b1, btop1), (b2, btop2)):
                sp.dma_start(to[:], of).then_inc(mlp_loaded, 16)
            with sp.Fori(0, PASSES) as h:
                for q in range(W_RING, QUADS + W_RING):
                    wait_low(sp, h, q - W_RING)
                    load_quad(q)
                    if q == 8:
                        sp.wait_ge(products, nth(h, DUOS + 2 - SLOTS, SLOTS))
                        sp.dma_start(zs[:], dense_rows[bass.ds(h, 1)].rearrange("o p b c -> (o p) b c")
                                     ).then_inc(dense_loaded, 16)
            sp.wait_ge(mlp_drained, MLP_DUOS * (PASSES + 1))
            sp.dma_start(out, ys[:]).then_inc(y_stored, 16)
            sp.wait_ge(y_stored, 16)

        @block.gpsimd
        def _(pool):
            pool.wait_ge(ids_loaded, 16)

            def gather(h, j, c, f):
                if not c and not f:
                    used = j + 1 - ROWS_RING
                    if h == 0 and table_slot <= j < ROWS_RING:
                        used = (j - table_slot) // 2 + 1
                    pool.wait_ge(transposed, nth(h, used, COUPLES))
                n = ((h * COUPLES + j) * CHUNKS + c) * 2 + f
                pool.indirect_dma_start(
                    rows[:, j % ROWS_RING, c, f * EMBED:(f + 1) * EMBED], None, tables[2 * j + f],
                    bass.IndirectOffsetOnAxis(ap=idx[:, n:n + 1].bitcast(u32), axis=0),
                ).then_inc(gathered[j], 16)

            def low_halves_of_quad(h, q):
                pool.wait_ge(w_high, nth(h, q + 1, QUADS))
                nc.gpsimd.tensor_tensor(wlow[:, q % S_RING, :], wraw[:, q % W_RING, :],
                                        whigh[:, q % S_RING, :].bitcast(f32), ALU.subtract
                                        ).then_inc(w_ready[q % S_RING], 1)

            for step in pool_order():
                if len(step) == 2:
                    low_halves_of_quad(*step)
                else:
                    gather(*step)

        @block.scalar
        def _(act):
            act.sem_inc(w_high, QUADS)
            act.sem_inc(x_high, COUPLES)
            act.sem_inc(mlp_drained, MLP_DUOS)

            def duos_before(n):
                return n if n > 0 else n - MLP_DUOS

            def high_halves_of_quad(h, q):
                slot = q % W_RING
                act.wait_ge(raw_loaded[slot], h * (32 * QUADS // W_RING) + 32 * (q // W_RING + 1))
                act.wait_ge(products, nth(h, duos_before(2 * (q - S_RING) + 2), SLOTS))
                nc.scalar.activation(whigh[:, q % S_RING, :], wraw[:, slot, :], ACT.Copy).then_inc(w_high, 1)

            def high_halves_of_couple(h, j):
                past, of = divmod(j, COUPLES)
                act.wait_ge(transposed, nth(h, j + 1, COUPLES))
                if j >= Q_RING:
                    act.wait_ge(drained, nth(h, first_duo(j - Q_RING + 1) + 1, DUOS))
                else:
                    act.wait_ge(drained, nth(h, 0, DUOS))
                nc.scalar.activation(qs[:, j % Q_RING, :], tps[:], ACT.Copy)
                last = ((COUPLES - 1) ** 2 + min(2 * of + 1, 2 * COUPLES - 2)) // 2 + 1
                act.wait_ge(products, nth(h, last + (past - 1) * SLOTS, SLOTS))
                for f in range(2):
                    a = EMBED * f
                    done = nc.scalar.activation(xs[a:a + EMBED, 2 * of + f, :], tps[a:a + EMBED, :], ACT.Copy)
                done.then_inc(x_high, 1)

            def relu_duo(h, n, to, bias):
                act.wait_ge(products, nth(h, DUOS + n + 1, SLOTS))
                for m in range(2):
                    at = (DUOS + n) % PS_BUFS * 2 + m
                    done = nc.scalar.activation(to[:, m, :], pbuf[:, at, :], ACT.Relu, bias=bias[:, m:m + 1])
                done.then_inc(mlp_drained, 1)

            for q in range(S_RING - 1):
                high_halves_of_quad(0, q)
            for j in range(AHEAD):
                high_halves_of_couple(0, j)
            high_halves_of_quad(0, S_RING - 1)
            act.wait_ge(mlp_loaded, 5 * 16)
            with act.Fori(0, PASSES) as h:
                for q in range(S_RING, QUADS + S_RING):
                    for d in (2 * (q - S_RING), 2 * (q - S_RING) + 1):
                        for j in couples_at(d):
                            high_halves_of_couple(h, j)
                    high_halves_of_quad(h, q)
                relu_duo(h, 0, h1s[:, 0:2, :], b1[:, 0:2])
                relu_duo(h, 1, h1s[:, 2:4, :], b1[:, 2:4])
                relu_duo(h, 2, h2s, b2)
                act.wait_ge(products, nth(h, SLOTS, SLOTS))
                nc.scalar.activation(ys[:, bass.ds(h * COLS, COLS)], pbuf[0:1, (SLOTS - 1) % PS_BUFS * 2, :],
                                     ACT.Copy).then_inc(mlp_drained, 1)

        @block.vector
        def _(dve):
            dve.sem_inc(x_ready, COUPLES)
            for slot in range(S_RING):
                dve.sem_inc(w_ready[slot], QUADS // S_RING)
            dve.sem_inc(drained, DUOS)
            dve.sem_inc(z_ready, BLOCKS)

            def low_halves_of_quad(h, q):
                dve.wait_ge(w_high, nth(h, q + 1, QUADS))
                nc.vector.tensor_tensor(wlow[:, q % S_RING, :], wraw[:, q % W_RING, :],
                                        whigh[:, q % S_RING, :].bitcast(f32), ALU.subtract).then_inc(w_ready[q % S_RING], 1)

            def low_halves_of_fields(h, j, fields=(0, 1)):
                dve.wait_ge(x_high, nth(h, j + 1, COUPLES))
                for f in fields:
                    a, b = EMBED * f, EMBED * (1 - f)
                    i = (2 * j + f) % FIELDS
                    done = nc.vector.tensor_tensor(xs[b:b + EMBED, i, :], tps[a:a + EMBED, :],
                                                   xs[a:a + EMBED, i, :].bitcast(f32), ALU.subtract)
                if 1 in fields:
                    done.then_inc(x_ready, 1)

            on_pool_quads = {step for step in pool_order() if len(step) == 2}

            def on_pool(h, q):
                h, q = h + q // QUADS, q % QUADS
                return (h, q) in on_pool_quads

            def multiply_duo(h, d):
                dve.wait_ge(products, nth(h, d + 1, SLOTS))
                dve.wait_ge(summed, nth(h, d // 2 + 1 - PROD_RING, QUADS))
                at, to = d % PS_BUFS * 2, d % (2 * PROD_RING) * 2
                ja, jb = tile_of(2 * d)[1] % Q_RING, tile_of(2 * d + 1)[1] % Q_RING
                if ja == jb:
                    q = qs[:, ja:ja + 1, :].to_broadcast([P, 2, COLS])
                    nc.vector.tensor_tensor(prod[:, to:to + 2, :], pbuf[:, at:at + 2, :], q,
                                            ALU.mult).then_inc(drained, 1)
                else:
                    nc.vector.tensor_tensor(prod[:, to, :], pbuf[:, at, :], qs[:, ja, :], ALU.mult)
                    nc.vector.tensor_tensor(prod[:, to + 1, :], pbuf[:, at + 1, :], qs[:, jb, :],
                                            ALU.mult).then_inc(drained, 1)

            def keep_block(h, b):
                dve.wait_ge(summed, nth(h, BLOCK * (b + 1), QUADS))
                if b == 0:
                    dve.wait_ge(dense_loaded, h * 16 + 16)
                nc.vector.tensor_tensor(zs[:, b, :], zacc[:], zs[:, b, :], ALU.add).then_inc(z_ready, 1)

            dve.wait_ge(numbers_loaded, 16)

            def one_hot_of_field(n):
                dve.wait_ge(small_loaded[n], 2 * 16)
                for t in range(K_TILES):
                    if n and n % 2 == 0 and t == K_TILES - 1:
                        dve.wait_ge(transposed, nth(0, n // 2, COUPLES))
                    elif n:
                        dve.wait_ge(looked_up, (n - 1) * K_TILES + t + 1 - (n - 1) // 2)
                    nc.vector.tensor_scalar(prod[0:K_ROWS, t, :], first_ids[0:K_ROWS, n, :],
                                            numbers[0:K_ROWS, t:t + 1], None, ALU.is_equal).then_inc(one_hot, 1)

            one_hot_of_field(0)
            low_halves_of_quad(0, 0)
            one_hot_of_field(1)
            for j in range(AHEAD):
                if j + 1 < AHEAD:
                    one_hot_of_field(2 * j + 2)
                low_halves_of_fields(0, j)
                if j + 1 < AHEAD:
                    one_hot_of_field(2 * j + 3)
            for q in range(1, S_RING):
                low_halves_of_quad(0, q)
            for h in range(PASSES):
                for d in range(DUOS):
                    for j in {0: couples_at(0), 1: []}.get(d, couples_at(d - 1)):
                        low_halves_of_fields(h, j, (0,) if j >= APART else (0, 1))
                    for j in couples_at(d - SECOND_FIELD):
                        if j >= APART:
                            low_halves_of_fields(h, j, (1,))
                    multiply_duo(h, d)
                    q = d // 2 + S_RING
                    if d % 2 and not on_pool(h, q):
                        low_halves_of_quad(h, q)
                    if d // 2 >= BLOCK and d % (2 * BLOCK) == 3:
                        keep_block(h, d // 2 // BLOCK - 1)
                keep_block(h, BLOCKS - 1)

        @block.tensor
        def _(pe):
            pe.sem_inc(transposed, COUPLES)
            pe.sem_inc(products, SLOTS)
            pe.sem_inc(summed, QUADS)

            def transpose_couple(h, j):
                gathers = 16 * 2 * CHUNKS
                if j < COUPLES:
                    pe.wait_ge(gathered[j], (h + 1) * gathers)
                else:
                    assert PASSES == 2 and j % COUPLES < AHEAD
                    pe.wait_ge(gathered[j % COUPLES], gathers)
                pe.wait_ge(x_ready, nth(h, j, COUPLES))
                for c in range(CHUNKS):
                    done = nc.tensor.transpose(tps[:, c * P:(c + 1) * P], rows[:, j % ROWS_RING, c, :], ident[:])
                done.then_inc(transposed, 1)

            def buffer_is_free(h, slot):
                last = slot - PS_BUFS
                if 0 <= last < DUOS:
                    pe.wait_ge(drained, nth(h, last + 1, DUOS))
                elif last < 0:
                    pe.wait_ge(mlp_drained, nth(h, last + 1, MLP_DUOS))
                else:
                    pe.wait_ge(mlp_drained, nth(h, last + 1 - DUOS, MLP_DUOS))

            def look_up_couple(j):
                pe.wait_ge(x_ready, nth(0, j, COUPLES))
                for f in range(2):
                    n = 2 * j + f
                    table = rows[0:K_ROWS, table_slot + n, :, :].rearrange("p a b -> p (a b)")
                    for t in range(K_TILES):
                        pe.wait_ge(one_hot, n * K_TILES + t + 1)
                        done = nc.tensor.matmul(tps[EMBED * f:EMBED * (f + 1), :],
                                                table[:, t * EMBED:(t + 1) * EMBED],
                                                prod[0:K_ROWS, t, :], start=(t == 0), stop=(t == K_TILES - 1))
                        done.then_inc(transposed if f and t == K_TILES - 1 else looked_up, 1)

            def products_of_duo(h, d):
                if d % 2 == 0:
                    wait_low(pe, h, d // 2)
                buffer_is_free(h, d)
                for t in range(2 * d, 2 * d + 2):
                    i, j = tile_of(t)
                    if i == 2 * j:
                        pe.wait_ge(x_ready, nth(h, j + 1, COUPLES))
                    at = slice(t % QUAD * P, (t % QUAD + 1) * P)
                    to = pbuf[:, d % PS_BUFS * 2 + t % 2, :]
                    nc.tensor.matmul(to, whigh[:, t // QUAD % S_RING, at], xs[:, i, :], start=True, stop=False)
                    done = nc.tensor.matmul(to, wlow[:, t // QUAD % S_RING, at], xs[:, i, :],
                                            start=False, stop=True)
                done.then_inc(products, 1)

            def sum_quad(h, q):
                pe.wait_ge(drained, nth(h, 2 * q + 2, DUOS))
                k = q % BLOCK
                if k == 0:
                    pe.wait_ge(z_ready, nth(h, q // BLOCK, BLOCKS))
                for g in range(QUAD):
                    done = nc.tensor.matmul(zacc[32 * g:32 * (g + 1), :], window[:, 30 - 2 * k:62 - 2 * k],
                                            prod[:, q % PROD_RING * QUAD + g, :],
                                            start=(k == 0), stop=(k == BLOCK - 1))
                done.then_inc(summed, 1)

            def layer(n, m, weights, inputs, kbs, first, last):
                for kb in kbs:
                    done = nc.tensor.matmul(pbuf[:, (DUOS + n) % PS_BUFS * 2 + m % 2, :],
                                            weights[:, kb, m * P:(m + 1) * P], inputs[:, kb, :],
                                            start=(kb == first), stop=(kb == last))
                return done

            for j in range(AHEAD):
                look_up_couple(j)
            pe.wait_ge(consts_loaded, 2 * 16)
            with pe.Fori(0, PASSES) as h:
                for d in range(DUOS):
                    for j in couples_at(d):
                        transpose_couple(h, j)
                    products_of_duo(h, d)
                    q = d // 2
                    if d % 2 and q > SUM_QUADS and q % SUM_QUADS:
                        for n in range(q - SUM_QUADS - 1, q - 1):
                            sum_quad(h, n)
                last = BLOCKS - 1
                buffer_is_free(h, DUOS)
                pe.wait_ge(z_ready, nth(h, last, BLOCKS))
                pe.wait_ge(mlp_loaded, 5 * 16)
                for m in range(2):
                    layer(0, m, wt1, zs, range(last), 0, last)
                for n in range(QUADS - SUM_QUADS, QUADS):
                    sum_quad(h, n)
                buffer_is_free(h, DUOS + 1)
                for m in range(2, 4):
                    layer(1, m, wt1, zs, range(last), 0, last)
                pe.wait_ge(z_ready, nth(h, BLOCKS, BLOCKS))
                for n in range(2):
                    for m in range(2 * n, 2 * n + 2):
                        done = layer(n, m, wt1, zs, [last], 0, last)
                    done.then_inc(products, 1)
                buffer_is_free(h, DUOS + 2)
                pe.wait_ge(mlp_drained, nth(h, 1, MLP_DUOS))
                for m in range(2):
                    layer(2, m, wt2, h1s, [0, 1], 0, 3)
                pe.wait_ge(mlp_drained, nth(h, 2, MLP_DUOS))
                for m in range(2):
                    done = layer(2, m, wt2, h1s, [2, 3], 0, 3)
                done.then_inc(products, 1)
                pe.wait_ge(mlp_drained, nth(h, 3, MLP_DUOS))
                for kb in range(2):
                    done = nc.tensor.matmul(pbuf[0:1, (SLOTS - 1) % PS_BUFS * 2, :], wt3[:, kb:kb + 1],
                                            h2s[:, kb, :], start=(kb == 0), stop=(kb == 1))
                done.then_inc(products, 1)


def kernel(**inputs):
    import numpy as np
    import concourse.bacc as bacc
    from concourse import mybir as mb
    from concourse.bass_utils import run_bass_kernel_spmd

    w = np.asarray(inputs["L0_rec_w"])
    ids = np.asarray(inputs["ids"])
    dense = np.asarray(inputs["dense_ctx"])
    wtop1 = np.asarray(inputs["W_top1"])
    number, n = {}, 0
    for i in range(FIELDS - 1):
        for j in range(i + 1, FIELDS):
            number[i, j] = n
            n += 1

    def pair(a, b):
        i, j = ORDER[a], ORDER[b]
        return (number[i, j], w[number[i, j]]) if i < j else (number[j, i], w[number[j, i]].T)

    wtiles = np.zeros((QUADS, EMBED, QUAD, 2, EMBED), np.float32)
    wt1 = np.zeros((P, BLOCKS, H1), np.float32)
    dense_rows = np.zeros((PASSES, P, BLOCKS, COLS), np.float32)
    for t in range(TILES):
        i, j = tile_of(t)
        q, g = t // QUAD, t % QUAD
        for s in range(2):
            row, b = 32 * g + 2 * (q % BLOCK) + s, q // BLOCK
            if 2 * j + s > i:
                n, weights = pair(i, 2 * j + s)
                wtiles[q, :, g, s] = weights
                wt1[row, b] = wtop1[n]
            else:
                wt1[row, b] = wtop1[PAIRS + j]
                for h in range(PASSES):
                    dense_rows[h, row, b] = dense[h * COLS:(h + 1) * COLS, j]
    window = np.zeros((P, 62), np.float32)
    window[:EMBED, 30] = 1
    window[EMBED:, 31] = 1
    arrays = {
        "ids_d": ids[:, ORDER].reshape(PASSES, CHUNKS, P, COUPLES, 2).transpose(2, 0, 3, 1, 4).reshape(P, -1),
        "wtiles_d": wtiles.reshape(QUADS, EMBED, QUAD * P),
        "wtop1_d": wt1,
        "btop1_d": np.asarray(inputs["b_top1"]).reshape(H1 // P, P).T,
        "wtop2_d": np.asarray(inputs["W_top2"]).reshape(H1 // P, P, H2).transpose(1, 0, 2),
        "btop2_d": np.asarray(inputs["b_top2"]).reshape(H2 // P, P).T,
        "wtop3_d": np.asarray(inputs["W_top3"]).reshape(H2 // P, P).T,
        "dense_d": dense_rows,
        "eye_d": np.eye(P, dtype=np.float32),
        "window_d": window,
        "small_ids_d": ids[:COLS, SMALL].T,
        "numbers_d": np.arange(P * K_TILES, dtype=np.float32).reshape(P, K_TILES),
    }
    for f in range(FIELDS):
        arrays[f"tbl_{f}_d"] = np.asarray(inputs[f"tbl_{f}"])
    arrays = {k: np.ascontiguousarray(v) for k, v in arrays.items()}

    nc = bacc.Bacc("TRN2", target_bir_lowering=False, num_devices=1)
    ap = {k: nc.dram_tensor(k, v.shape, mb.dt.from_np(v.dtype), kind="ExternalInput").ap()
          for k, v in arrays.items()}
    out = nc.dram_tensor("y_d", (1, BATCH), mb.dt.float32, kind="ExternalOutput").ap()
    build(nc, out, ap["ids_d"], [ap[f"tbl_{f}_d"] for f in ORDER], ap["wtiles_d"], ap["wtop1_d"],
          ap["btop1_d"], ap["wtop2_d"], ap["btop2_d"], ap["wtop3_d"], ap["dense_d"], ap["eye_d"],
          ap["window_d"], ap["small_ids_d"], ap["numbers_d"])
    r = run_bass_kernel_spmd(nc, [arrays], core_ids=[0])
    return r.results[0]["y_d"].reshape(BATCH, 1)
```

```python
from contextlib import ExitStack

import concourse.bass as bass
from concourse import mybir

FIELDS, EMBED, BATCH, DENSE = 32, 64, 1024, 16
PAIRS = FIELDS * (FIELDS - 1) // 2
P = 128
COLS = 512
PASSES = BATCH // COLS
CHUNKS = COLS // P
COUPLES = FIELDS // 2
QUAD = 4
BLOCK = 16
H1, H2 = 512, 256
MLP_DUOS = 4
PS_BUFS = 3
RING = 4
Q_RING = 4
ROWS_RING = 8
SUM_QUADS = 2
LOOKAHEAD = 2
LOOKED_UP = 2
AHEAD = 4
AHEAD_MLP = 2
APART = 6
K_ROWS, K_TILES = 125, 8

SMALL = [0, 1, 2, 7]
ORDER = SMALL + [f for f in range(FIELDS) if f not in SMALL]


def all_tiles():
    tiles = []
    for a in range(0, FIELDS, 4):
        b, c, d, first, second = a + 1, a + 2, a + 3, a // 2, a // 2 + 1
        tiles += [(first, i, a, b) for i in range(a)]
        tiles += [(second, i, c, d) for i in range(a)]
        plain, special = [(second, b, c, d)], [(second, d, a, c), (second, a, c, b)]
        tiles += special + plain if len(tiles) % 2 == 0 else plain + special
    return tiles


TILES = all_tiles()
DUOS = len(TILES) // 2
QUADS = len(TILES) // QUAD
BLOCKS = -(-QUADS // BLOCK)
SLOTS = DUOS + MLP_DUOS


def first_duo(j):
    return min(t for t, tile in enumerate(TILES) if tile[0] >= j) // 2


def last_q_duo(j):
    return max(t for t, tile in enumerate(TILES) if j in (tile[2] // 2, tile[3] // 2)) // 2


def last_x_duo(j):
    return max(t for t, tile in enumerate(TILES) if tile[1] // 2 == j) // 2


def couples_at(d):
    at = {j: max(0, first_duo(j) - LOOKAHEAD) for j in range(AHEAD, COUPLES)}
    for n in range(AHEAD - AHEAD_MLP):
        at[COUPLES + n] = DUOS - 4 * (AHEAD - AHEAD_MLP - n)
    return [j for j in at if at[j] == d]


def lows_at(d):
    at = {}
    for t in range(DUOS):
        for j in couples_at(t):
            after = (0, 3) if APART <= j < COUPLES else (0, 0)
            for f in range(2):
                at[j, f] = t + after[f] + 1
                if APART <= j < COUPLES and at[j, f] % 2 == 0:
                    at[j, f] += 1
    return [field for field in at if at[field] == d]


def slot_of(q):
    return q % QUADS % RING


def uses(slot):
    return (QUADS - slot + RING - 1) // RING


def quad_before(q):
    return q - RING if q < QUADS else max(n for n in range(QUADS) if n % RING == slot_of(q))


def buffer_of(slot):
    return slot % PS_BUFS * 2


def nth(h, n, per_pass):
    return h * per_pass + (per_pass + n)


def pool_order():
    gather_us, low_us, quad_us, mlp_us, start = 1.04, 1.25, 2.9, 22.0, 22.0
    margin_low, margin_gather = 2.0, 4.0

    def at(h, q):
        early = lambda n: 0.6 * min(n, 8)
        return start + quad_us * q + early(q) + (QUADS * quad_us + early(QUADS) + mlp_us) * h

    gathers = [(h, j, c, f) for h in range(PASSES) for j in range(LOOKED_UP * (h == 0), COUPLES)
               for c in range(CHUNKS) for f in range(2)]

    def spare(now):
        least = 1e9
        for n, (h, j, c, f) in enumerate(gathers):
            if c == CHUNKS - 1 and f:
                early = (first_duo(j) - LOOKAHEAD) / 2 if j >= AHEAD else 2 * j - 2 * AHEAD
                least = min(least, at(h, early) - margin_gather - now - (n + 1) * gather_us)
        return least

    def slot_free():
        h, j = gathers[0][:2]
        past = COUPLES * h + j - ROWS_RING
        if past < AHEAD:
            return 0
        if past < COUPLES + AHEAD:
            return at(0, (first_duo(past) - LOOKAHEAD) / 2 if past < COUPLES else QUADS)
        return at(1, (first_duo(past - COUPLES) - LOOKAHEAD) / 2)

    order, now, quad = [], 0.0, RING
    while gathers or quad < PASSES * QUADS:
        h, q = divmod(quad, QUADS)
        if h < PASSES and now + low_us > at(h, q) - margin_low:
            quad += 1
        elif h < PASSES and now >= at(h, q - RING) + 2 and spare(now) > low_us:
            order.append((h, q))
            now += low_us
            quad += 1
        elif gathers and now >= slot_free():
            order.append(gathers.pop(0))
            now += gather_us
        else:
            now += 0.5
    return order


def build(nc, out, ids, tables, wtiles, wtop1, btop1, wtop2, btop2, wtop3, dense_rows, eye, ones,
          small_ids, row_numbers):
    f32, f32r, i32 = mybir.dt.float32, mybir.dt.float32r, mybir.dt.int32
    u32 = mybir.dt.uint32
    ALU = mybir.AluOpType
    ACT = mybir.ActivationFunctionType
    ctx = ExitStack()
    with ctx:
        def sb(name, shape, dt=f32):
            return ctx.enter_context(nc.sbuf_tensor(name, shape, dt))

        def ps(name, shape):
            return ctx.enter_context(nc.psum_tensor(name, shape, f32))

        def sem(name):
            return ctx.enter_context(nc.semaphore(name))

        rows = sb("rows", [P, ROWS_RING, CHUNKS, 2 * EMBED])
        xs = sb("xs", [P, FIELDS, COLS], f32r)
        qs = sb("qs", [P, Q_RING, COLS])
        wraw = sb("wraw", [P, RING, QUAD * P])
        whigh = sb("whigh", [P, RING, QUAD * P], f32r)
        wlow = sb("wlow", [P, RING, QUAD * P], f32r)
        prod = sb("prod", [P, RING * QUAD, COLS])
        zs = sb("zs", [P, BLOCKS, COLS])
        h1s = sb("h1s", [P, H1 // P, COLS])
        h2s = sb("h2s", [P, H2 // P, COLS])
        ys = sb("ys", [1, BATCH])
        wt1 = sb("wt1", [P, BLOCKS, H1])
        wt2 = sb("wt2", [P, H1 // P, H2])
        wt3 = sb("wt3", [P, H2 // P])
        b1 = sb("b1", [P, H1 // P])
        b2 = sb("b2", [P, H2 // P])
        idx = sb("idx", [P, PASSES * COUPLES * CHUNKS * 2], i32)
        ident = sb("ident", [P, P])
        window = sb("window", [P, 62])
        first_ids = h1s[:, :, :].bitcast(i32)
        numbers = sb("numbers", [P, K_TILES])
        table_slot = ROWS_RING - 2 * LOOKED_UP

        pbuf = ps("pbuf", [P, 2 * PS_BUFS, COLS])
        zacc = ps("zacc", [P, COLS])
        tps = ps("tps", [P, COLS])

        ids_loaded = sem("ids_loaded")
        numbers_loaded = sem("numbers_loaded")
        small_loaded = [sem(f"small_loaded{n}") for n in range(2 * LOOKED_UP)]
        consts_loaded = sem("consts_loaded")
        mlp_loaded = sem("mlp_loaded")
        one_hot = sem("one_hot")
        looked_up = sem("looked_up")
        gathered = [sem(f"gathered{j}") for j in range(COUPLES)]
        raw_loaded = [sem(f"raw_loaded{s}") for s in range(RING)]
        transposed = sem("transposed")
        x_high = sem("x_high")
        x_ready = sem("x_ready")
        w_high = sem("w_high")
        w_ready = [sem(f"w_ready{s}") for s in range(RING)]
        products = sem("products")
        drained = sem("drained")
        mlp_drained = sem("mlp_drained")
        summed = sem("summed")
        z_ready = sem("z_ready")
        dense_loaded = sem("dense_loaded")
        y_stored = sem("y_stored")

        def wait_low(eng, h, q):
            past, of = divmod(q, QUADS)
            per_pass = uses(slot_of(q))
            eng.wait_ge(w_ready[slot_of(q)], nth(h, past * per_pass + of // RING + 1, per_pass))

        def table_of(n):
            return rows[0:K_ROWS, table_slot + n, :, :].rearrange("p a b -> p (a b)")

        def transposed_bank(prologue, j):
            return zacc if prologue and j % 2 else tps

        block = ctx.enter_context(nc.Block())

        @block.sync
        def _(sp):
            def load_quad(q):
                for half in range(2):
                    sp.dma_start(wraw[EMBED * half:EMBED * (half + 1), slot_of(q), :],
                                 wtiles[q % QUADS]).then_inc(raw_loaded[slot_of(q)], 16)

            sp.dma_start(idx[:], ids).then_inc(ids_loaded, 16)
            sp.dma_start(numbers[:], row_numbers).then_inc(numbers_loaded, 16)
            for n in range(2 * LOOKED_UP):
                sp.dma_start(first_ids[:, n, :], small_ids[n:n + 1].to_broadcast([P, COLS])
                             ).then_inc(small_loaded[n], 16)
                sp.dma_start(table_of(n), tables[n].rearrange("(p t) e -> p (t e)", t=K_TILES)
                             ).then_inc(small_loaded[n], 16)
            for q in range(RING):
                load_quad(q)
            sp.dma_start(ident[:], eye).then_inc(consts_loaded, 16)
            sp.dma_start(window[:], ones).then_inc(consts_loaded, 16)
            for to, of in ((wt1, wtop1), (wt2, wtop2), (wt3, wtop3), (b1, btop1), (b2, btop2)):
                sp.dma_start(to[:], of).then_inc(mlp_loaded, 16)
            with sp.Fori(0, PASSES) as h:
                for q in range(RING, QUADS + RING):
                    wait_low(sp, h, quad_before(q))
                    load_quad(q)
                    if q == 8:
                        sp.wait_ge(products, nth(h, 2 - MLP_DUOS, SLOTS))
                        sp.dma_start(zs[:], dense_rows[bass.ds(h, 1)].rearrange("o p b c -> (o p) b c")
                                     ).then_inc(dense_loaded, 16)
            sp.wait_ge(mlp_drained, MLP_DUOS * (PASSES + 1))
            sp.dma_start(out, ys[:]).then_inc(y_stored, 16)
            sp.wait_ge(y_stored, 16)

        @block.gpsimd
        def _(pool):
            pool.wait_ge(ids_loaded, 16)

            def gather(h, j, c, f):
                if not c and not f:
                    used = j + 1 - ROWS_RING
                    if h == 0 and table_slot <= j < ROWS_RING:
                        used = (j - table_slot) // 2 + 1
                    pool.wait_ge(transposed, nth(h, used, COUPLES))
                n = ((h * COUPLES + j) * CHUNKS + c) * 2 + f
                pool.indirect_dma_start(
                    rows[:, j % ROWS_RING, c, f * EMBED:(f + 1) * EMBED], None, tables[2 * j + f],
                    bass.IndirectOffsetOnAxis(ap=idx[:, n:n + 1].bitcast(u32), axis=0),
                ).then_inc(gathered[j], 16)

            def low_halves_of_quad(h, q):
                pool.wait_ge(w_high, nth(h, q + 1, QUADS))
                nc.gpsimd.tensor_tensor(wlow[:, slot_of(q), :], wraw[:, slot_of(q), :],
                                        whigh[:, slot_of(q), :].bitcast(f32), ALU.subtract
                                        ).then_inc(w_ready[slot_of(q)], 1)

            for step in pool_order():
                if len(step) == 2:
                    low_halves_of_quad(*step)
                else:
                    gather(*step)

        @block.scalar
        def _(act):
            act.sem_inc(w_high, QUADS)
            act.sem_inc(x_high, COUPLES)
            act.sem_inc(mlp_drained, MLP_DUOS)

            def high_halves_of_quad(h, q):
                past, of = divmod(q, QUADS)
                n = past * uses(slot_of(q)) + of // RING + 1
                act.wait_ge(raw_loaded[slot_of(q)], h * (32 * uses(slot_of(q))) + 32 * n)
                if q >= RING:
                    act.wait_ge(products, nth(h, 2 * quad_before(q) + 2, SLOTS))
                nc.scalar.activation(whigh[:, slot_of(q), :], wraw[:, slot_of(q), :], ACT.Copy
                                     ).then_inc(w_high, 1)

            def high_halves_of_couple(h, j, prologue=False):
                past, of = divmod(j, COUPLES)
                act.wait_ge(transposed, nth(h, j + 1, COUPLES))
                act.wait_ge(drained, nth(h, last_q_duo(j - Q_RING) + 1 if j >= Q_RING else 0, DUOS))
                bank = transposed_bank(prologue, j)
                nc.scalar.activation(qs[:, j % Q_RING, :], bank[:], ACT.Copy)
                act.wait_ge(products, nth(h, last_x_duo(of) + 1 + (past - 1) * SLOTS, SLOTS))
                for f in range(2):
                    a = EMBED * f
                    done = nc.scalar.activation(xs[a:a + EMBED, 2 * of + f, :], bank[a:a + EMBED, :], ACT.Copy)
                done.then_inc(x_high, 1)

            def relu_duo(h, n, to, bias):
                act.wait_ge(products, nth(h, DUOS + n + 1, SLOTS))
                for m in range(2):
                    done = nc.scalar.activation(to[:, m, :], pbuf[:, buffer_of(DUOS + n) + m, :],
                                                ACT.Relu, bias=bias[:, m:m + 1])
                done.then_inc(mlp_drained, 1)

            for q in range(RING - 1):
                high_halves_of_quad(0, q)
            for j in range(LOOKED_UP):
                high_halves_of_couple(0, j, prologue=True)
            high_halves_of_quad(0, RING - 1)
            for j in range(LOOKED_UP, AHEAD):
                high_halves_of_couple(0, j, prologue=True)
            act.wait_ge(mlp_loaded, 5 * 16)
            with act.Fori(0, PASSES) as h:
                for d in range(DUOS):
                    for j in couples_at(d):
                        high_halves_of_couple(h, j)
                    if d % 2 and d // 2 + RING < QUADS:
                        high_halves_of_quad(h, d // 2 + RING)
                for q in range(QUADS, QUADS + RING):
                    high_halves_of_quad(h, q)
                for j in range(COUPLES + AHEAD - AHEAD_MLP, COUPLES + AHEAD):
                    high_halves_of_couple(h, j)
                relu_duo(h, 0, h1s[:, 0:2, :], b1[:, 0:2])
                relu_duo(h, 1, h1s[:, 2:4, :], b1[:, 2:4])
                relu_duo(h, 2, h2s, b2)
                act.wait_ge(products, nth(h, SLOTS, SLOTS))
                nc.scalar.activation(ys[:, bass.ds(h * COLS, COLS)], pbuf[0:1, buffer_of(SLOTS - 1), :],
                                     ACT.Copy).then_inc(mlp_drained, 1)

        @block.vector
        def _(dve):
            dve.sem_inc(x_ready, COUPLES)
            for slot in range(RING):
                dve.sem_inc(w_ready[slot], uses(slot))
            dve.sem_inc(drained, DUOS)
            dve.sem_inc(z_ready, BLOCKS)

            def one_hot_of_field(n):
                dve.wait_ge(small_loaded[n], 2 * 16)
                for t in range(K_TILES):
                    if n >= 2 and n % 2 == 0 and t == K_TILES - 1:
                        dve.wait_ge(transposed, nth(0, n // 2 - 1 + 1, COUPLES))
                    elif n >= 1:
                        dve.wait_ge(looked_up, (n - 1) * K_TILES + t + 1 - (n - 1) // 2)
                    nc.vector.tensor_scalar(prod[0:K_ROWS, t, :], first_ids[0:K_ROWS, n, :],
                                            numbers[0:K_ROWS, t:t + 1], None, ALU.is_equal
                                            ).then_inc(one_hot, 1)

            def low_halves_of_quad(h, q):
                dve.wait_ge(w_high, nth(h, q + 1, QUADS))
                nc.vector.tensor_tensor(wlow[:, slot_of(q), :], wraw[:, slot_of(q), :],
                                        whigh[:, slot_of(q), :].bitcast(f32), ALU.subtract
                                        ).then_inc(w_ready[slot_of(q)], 1)

            def low_halves_of_field(h, j, f, prologue=False):
                dve.wait_ge(x_high, nth(h, j + 1, COUPLES))
                a, b = EMBED * f, EMBED * (1 - f)
                i = (2 * j + f) % FIELDS
                done = nc.vector.tensor_tensor(xs[b:b + EMBED, i, :],
                                               transposed_bank(prologue, j)[a:a + EMBED, :],
                                               xs[a:a + EMBED, i, :].bitcast(f32), ALU.subtract)
                if f:
                    done.then_inc(x_ready, 1)

            def low_halves_of_couple(h, j, prologue=False):
                for f in range(2):
                    low_halves_of_field(h, j, f, prologue)

            def multiply_duo(h, d):
                dve.wait_ge(products, nth(h, d + 1, SLOTS))
                dve.wait_ge(summed, nth(h, max(0, d // 2 - RING + 1), QUADS))
                at, to = buffer_of(d), slot_of(d // 2) * QUAD + d % 2 * 2
                lower, upper = [[tile[k] for tile in TILES[2 * d:2 * d + 2]] for k in (2, 3)]
                slots = [x // 2 % Q_RING for x in lower]
                if all(u == x + 1 for x, u in zip(lower, upper)) and slots[0] == slots[1]:
                    q = qs[:, slots[0]:slots[0] + 1, :].to_broadcast([P, 2, COLS])
                    done = nc.vector.tensor_tensor(prod[:, to:to + 2, :], pbuf[:, at:at + 2, :], q, ALU.mult)
                elif all(u == x + 1 for x, u in zip(lower, upper)):
                    for n in range(2):
                        done = nc.vector.tensor_tensor(prod[:, to + n, :], pbuf[:, at + n, :],
                                                       qs[:, slots[n], :], ALU.mult)
                else:
                    assert slots[1] == slots[0] + 1
                    nc.vector.tensor_tensor(prod[0:EMBED, to:to + 2, :], pbuf[0:EMBED, at:at + 2, :],
                                            qs[0:EMBED, slots[0]:slots[0] + 2, :], ALU.mult)
                    for n in range(2):
                        a = upper[n] % 2 * EMBED
                        done = nc.vector.tensor_tensor(prod[EMBED:P, to + n, :], pbuf[EMBED:P, at + n, :],
                                                       qs[a:a + EMBED, upper[n] // 2 % Q_RING, :], ALU.mult)
                done.then_inc(drained, 1)

            def keep_block(h, b):
                dve.wait_ge(summed, nth(h, min(BLOCK * (b + 1), QUADS), QUADS))
                if b == 0:
                    dve.wait_ge(dense_loaded, h * 16 + 16)
                nc.vector.tensor_tensor(zs[:, b, :], zacc[:], zs[:, b, :], ALU.add).then_inc(z_ready, 1)

            dve.wait_ge(numbers_loaded, 16)
            one_hot_of_field(0)
            one_hot_of_field(1)
            low_halves_of_quad(0, 0)
            one_hot_of_field(2)
            low_halves_of_couple(0, 0, prologue=True)
            one_hot_of_field(3)
            low_halves_of_quad(0, 1)
            low_halves_of_couple(0, 1, prologue=True)
            for q in range(2, RING):
                low_halves_of_quad(0, q)
            for j in range(LOOKED_UP, AHEAD):
                low_halves_of_couple(0, j, prologue=True)
            on_pool = {step for step in pool_order() if len(step) == 2}
            for h in range(PASSES):
                for d in range(DUOS):
                    for j, f in lows_at(d):
                        low_halves_of_field(h, j, f)
                    multiply_duo(h, d)
                    q = d // 2 + RING
                    if d % 2 and q < QUADS and (h, q) not in on_pool:
                        low_halves_of_quad(h, q)
                    if d > 2 * BLOCK and d % (2 * BLOCK) == 3:
                        keep_block(h, d // (2 * BLOCK) - 1)
                for q in range(RING):
                    if (h + 1, q) not in on_pool:
                        low_halves_of_quad(h, QUADS + q)
                low_halves_of_couple(h, COUPLES + AHEAD - 2)
                keep_block(h, BLOCKS - 1)
                low_halves_of_couple(h, COUPLES + AHEAD - 1)

        @block.tensor
        def _(pe):
            pe.sem_inc(transposed, COUPLES)
            pe.sem_inc(products, SLOTS)
            pe.sem_inc(summed, QUADS)

            def look_up_couple(j):
                for f in range(2):
                    n = 2 * j + f
                    for t in range(K_TILES):
                        pe.wait_ge(one_hot, n * K_TILES + t + 1)
                        done = nc.tensor.matmul(transposed_bank(True, j)[EMBED * f:EMBED * (f + 1), :],
                                                table_of(n)[:, t * EMBED:(t + 1) * EMBED],
                                                prod[0:K_ROWS, t, :], start=(t == 0), stop=(t == K_TILES - 1))
                        done.then_inc(transposed if f and t == K_TILES - 1 else looked_up, 1)

            def transpose_couple(h, j, prologue=False):
                gathers = 16 * 2 * CHUNKS
                if j < COUPLES:
                    pe.wait_ge(gathered[j], (h + 1) * gathers)
                else:
                    assert PASSES == 2
                    pe.wait_ge(gathered[j % COUPLES], gathers * (1 if j % COUPLES < LOOKED_UP else 2))
                pe.wait_ge(x_ready, nth(h, j - prologue, COUPLES))
                for c in range(CHUNKS):
                    done = nc.tensor.transpose(transposed_bank(prologue, j)[:, c * P:(c + 1) * P],
                                               rows[:, j % ROWS_RING, c, :], ident[:])
                done.then_inc(transposed, 1)

            def buffer_is_free(h, slot):
                before = [n for n in range(slot - SLOTS, slot) if buffer_of(n % SLOTS) == buffer_of(slot)][-1]
                past, of = divmod(before, SLOTS)
                if of < DUOS:
                    pe.wait_ge(drained, nth(h, of + 1 + past * DUOS, DUOS))
                else:
                    pe.wait_ge(mlp_drained, nth(h, of - DUOS + 1 + past * MLP_DUOS, MLP_DUOS))

            def products_of_duo(h, d):
                if d % 2 == 0:
                    wait_low(pe, h, d // 2)
                buffer_is_free(h, d)
                for t in range(2 * d, 2 * d + 2):
                    i = TILES[t][1]
                    if i // 2 > max([tile[1] // 2 for tile in TILES[:t]], default=-1):
                        pe.wait_ge(x_ready, nth(h, i // 2 + 1, COUPLES))
                    at = slice(t % QUAD * P, (t % QUAD + 1) * P)
                    to = pbuf[:, buffer_of(d) + t % 2, :]
                    nc.tensor.matmul(to, whigh[:, slot_of(t // QUAD), at], xs[:, i, :], start=True, stop=False)
                    done = nc.tensor.matmul(to, wlow[:, slot_of(t // QUAD), at], xs[:, i, :],
                                            start=False, stop=True)
                done.then_inc(products, 1)

            def sum_quad(h, q):
                pe.wait_ge(drained, nth(h, 2 * q + 2, DUOS))
                k = q % BLOCK
                if k == 0:
                    pe.wait_ge(z_ready, nth(h, q // BLOCK, BLOCKS))
                for g in range(QUAD):
                    done = nc.tensor.matmul(zacc[32 * g:32 * (g + 1), :], window[:, 30 - 2 * k:62 - 2 * k],
                                            prod[:, slot_of(q) * QUAD + g, :], start=(k == 0),
                                            stop=(k == BLOCK - 1 or q == QUADS - 1))
                done.then_inc(summed, 1)

            def layer(n, m, weights, inputs, kbs, last):
                for kb in kbs:
                    done = nc.tensor.matmul(pbuf[:, buffer_of(DUOS + n) + m % 2, :],
                                            weights[:, kb, m * P:(m + 1) * P], inputs[:, kb, :],
                                            start=(kb == 0), stop=(kb == last))
                return done

            for j in range(LOOKED_UP):
                look_up_couple(j)
            pe.wait_ge(consts_loaded, 2 * 16)
            for j in range(LOOKED_UP, AHEAD):
                transpose_couple(0, j, prologue=True)
            with pe.Fori(0, PASSES) as h:
                for d in range(DUOS):
                    for j in couples_at(d):
                        transpose_couple(h, j)
                    products_of_duo(h, d)
                    q = d // 2
                    if d % 2 and q > SUM_QUADS and q % SUM_QUADS:
                        for n in range(q - SUM_QUADS - 1, q - 1):
                            sum_quad(h, n)
                transpose_couple(h, COUPLES + AHEAD - 2)
                last = BLOCKS - 1
                buffer_is_free(h, DUOS)
                pe.wait_ge(z_ready, nth(h, last, BLOCKS))
                pe.wait_ge(mlp_loaded, 5 * 16)
                for m in range(2):
                    layer(0, m, wt1, zs, range(last), last)
                for n in range(QUADS - SUM_QUADS, QUADS):
                    sum_quad(h, n)
                transpose_couple(h, COUPLES + AHEAD - 1)
                buffer_is_free(h, DUOS + 1)
                for m in range(2, 4):
                    layer(1, m, wt1, zs, range(last), last)
                pe.wait_ge(z_ready, nth(h, BLOCKS, BLOCKS))
                for n in range(2):
                    for m in range(2 * n, 2 * n + 2):
                        done = layer(n, m, wt1, zs, [last], last)
                    done.then_inc(products, 1)
                buffer_is_free(h, DUOS + 2)
                pe.wait_ge(mlp_drained, nth(h, 1, MLP_DUOS))
                for m in range(2):
                    layer(2, m, wt2, h1s, [0, 1], 3)
                pe.wait_ge(mlp_drained, nth(h, 2, MLP_DUOS))
                for m in range(2):
                    done = layer(2, m, wt2, h1s, [2, 3], 3)
                done.then_inc(products, 1)
                buffer_is_free(h, DUOS + 3)
                pe.wait_ge(mlp_drained, nth(h, 3, MLP_DUOS))
                for kb in range(2):
                    done = nc.tensor.matmul(pbuf[0:1, buffer_of(SLOTS - 1), :], wt3[:, kb:kb + 1],
                                            h2s[:, kb, :], start=(kb == 0), stop=(kb == 1))
                done.then_inc(products, 1)


def kernel(**inputs):
    import numpy as np
    import concourse.bacc as bacc
    from concourse import mybir as mb
    from concourse.bass_utils import run_bass_kernel_spmd

    w = np.asarray(inputs["L0_rec_w"])
    ids = np.asarray(inputs["ids"])
    dense = np.asarray(inputs["dense_ctx"])
    wtop1 = np.asarray(inputs["W_top1"])
    number, n = {}, 0
    for i in range(FIELDS - 1):
        for j in range(i + 1, FIELDS):
            number[i, j] = n
            n += 1

    def pair(a, b):
        i, j = ORDER[a], ORDER[b]
        return (number[i, j], w[number[i, j]]) if i < j else (number[j, i], w[number[j, i]].T)

    wtiles = np.zeros((QUADS, EMBED, QUAD, 2, EMBED), np.float32)
    wt1 = np.zeros((P, BLOCKS, H1), np.float32)
    dense_rows = np.zeros((PASSES, P, BLOCKS, COLS), np.float32)
    for t, (_, i, lower, upper) in enumerate(TILES):
        q, g = t // QUAD, t % QUAD
        for s, partner in enumerate((lower, upper)):
            n, weights = pair(i, partner)
            wtiles[q, :, g, s] = weights
            wt1[32 * g + 2 * (q % BLOCK) + s, q // BLOCK] = wtop1[n]
    free = [32 * g + r for g in range(QUAD) for r in range(2 * (QUADS - BLOCK * (BLOCKS - 1)), 32)]
    for n in range(DENSE):
        wt1[free[n], BLOCKS - 1] = wtop1[PAIRS + n]
        for h in range(PASSES):
            dense_rows[h, free[n], BLOCKS - 1] = dense[h * COLS:(h + 1) * COLS, n]
    window = np.zeros((P, 62), np.float32)
    window[:EMBED, 30] = 1
    window[EMBED:, 31] = 1
    arrays = {
        "ids_d": ids[:, ORDER].reshape(PASSES, CHUNKS, P, COUPLES, 2).transpose(2, 0, 3, 1, 4).reshape(P, -1),
        "wtiles_d": wtiles.reshape(QUADS, EMBED, QUAD * P),
        "wtop1_d": wt1,
        "btop1_d": np.asarray(inputs["b_top1"]).reshape(H1 // P, P).T,
        "wtop2_d": np.asarray(inputs["W_top2"]).reshape(H1 // P, P, H2).transpose(1, 0, 2),
        "btop2_d": np.asarray(inputs["b_top2"]).reshape(H2 // P, P).T,
        "wtop3_d": np.asarray(inputs["W_top3"]).reshape(H2 // P, P).T,
        "dense_d": dense_rows,
        "eye_d": np.eye(P, dtype=np.float32),
        "window_d": window,
        "small_ids_d": ids[:COLS, SMALL].T,
        "numbers_d": np.arange(P * K_TILES, dtype=np.float32).reshape(P, K_TILES),
    }
    for f in range(FIELDS):
        arrays[f"tbl_{f}_d"] = np.asarray(inputs[f"tbl_{f}"])
    arrays = {k: np.ascontiguousarray(v) for k, v in arrays.items()}

    nc = bacc.Bacc("TRN2", target_bir_lowering=False, num_devices=1)
    ap = {k: nc.dram_tensor(k, v.shape, mb.dt.from_np(v.dtype), kind="ExternalInput").ap()
          for k, v in arrays.items()}
    out = nc.dram_tensor("y_d", (1, BATCH), mb.dt.float32, kind="ExternalOutput").ap()
    build(nc, out, ap["ids_d"], [ap[f"tbl_{f}_d"] for f in ORDER], ap["wtiles_d"], ap["wtop1_d"],
          ap["btop1_d"], ap["wtop2_d"], ap["btop2_d"], ap["wtop3_d"], ap["dense_d"], ap["eye_d"],
          ap["window_d"], ap["small_ids_d"], ap["numbers_d"])
    r = run_bass_kernel_spmd(nc, [arrays], core_ids=[0])
    return r.results[0]["y_d"].reshape(BATCH, 1)
```
